# Optimizing a Trainium2 kernel written in Bass

```python
import numpy as np
import jax
import jax.numpy as jnp

def _softmax(x, axis=-1):
    return jax.nn.softmax(x, axis=axis)

def _gelu(x):
    return jax.nn.gelu(x, approximate=True)

def _silu(x):
    return jax.nn.silu(x)

def _sigmoid(x):
    return jax.nn.sigmoid(x)

def _layernorm(x, axis=-1, eps=1e-05):
    m = jnp.mean(x, axis=axis, keepdims=True)
    v = jnp.var(x, axis=axis, keepdims=True)
    return (x - m) / jnp.sqrt(v + eps)

def _scatter_add(tgt, idx, src, axis=0):
    return tgt.at[idx].add(src)

def _segment_sum(src, seg, n):
    return jax.ops.segment_sum(src, seg, n)
kernel_name = 'mk_adj_resnorm_d4_adj_r2_26718a'

def setup_inputs(seed: int=0):
    np.random.seed(seed)
    _w = jnp.asarray

    def _rec_inputs():
        import jax
        import jax.numpy as jnp
        _gk = jax.random.key(seed)
        x = 0.0001732 + 1 * jax.random.normal(jax.random.fold_in(_gk, 1), (5120, 64), jnp.float32)
        _a = jax.random.bernoulli(jax.random.fold_in(_gk, 2), 0.0015625, (5120, 5120))
        _af = _a.astype(jnp.float32)
        _af = _af * jax.random.uniform(jax.random.fold_in(_gk, 3), (5120, 5120), jnp.float32, 0.05, 0.02)
        adj = _af
        return (x, adj)
    x, adj = _rec_inputs()

    def _L0_gnn_setup():
        import jax, jax.numpy as jnp
        import numpy as np
        N_USERS = 2048
        N_ITEMS = 3072
        EMB = 64
        LN_EPS = 1e-05
        key = jax.random.key(seed)
        ks = jax.random.split(key, 10)
        N = N_USERS + N_ITEMS
        ego = jax.random.normal(ks[0], (N, EMB), jnp.float32)
        adj = (jax.random.uniform(ks[1], (N, N), jnp.float32) < 0.01).astype(jnp.float32) * 0.02
        xav = float(np.sqrt(6.0 / (EMB + EMB)))
        W_u = jax.random.uniform(ks[2], (EMB, EMB), jnp.float32, -xav, xav)
        W_i = jax.random.uniform(ks[3], (EMB, EMB), jnp.float32, -xav, xav)
        diag_u = jax.random.uniform(ks[4], (N_USERS,), jnp.float32, 0.99, 1.01)
        diag_i = jax.random.uniform(ks[5], (N_ITEMS,), jnp.float32, 0.99, 1.01)
        par_u = jax.random.uniform(ks[6], (2,), jnp.float32, 0.0, 0.99)
        par_i = jax.random.uniform(ks[7], (2,), jnp.float32, 0.0, 0.99)
        ln_gamma = jnp.ones((EMB,), jnp.float32)
        ln_beta = jnp.zeros((EMB,), jnp.float32)
        return {'ego_embeddings': ego, 'adj': adj, 'W_u': W_u, 'diag_u': diag_u, 'par_u': par_u, 'W_i': W_i, 'diag_i': diag_i, 'par_i': par_i, 'ln_gamma': ln_gamma, 'ln_beta': ln_beta}
    _L0_gnn_all = _L0_gnn_setup()
    _L0_gnn_in = {k: v for k, v in _L0_gnn_all.items() if k in ('W_u', 'diag_u', 'par_u', 'W_i', 'diag_i', 'par_i', 'ln_gamma', 'ln_beta')}
    del _L0_gnn_all

    def _L1_gnn_setup():
        import jax, jax.numpy as jnp
        import numpy as np
        N = 4096
        DIN = 64
        DH = 64
        DOUT = 64
        SPARSITY = 0.01
        key = jax.random.key(seed)
        ks = jax.random.split(key, 9)
        x = jax.random.normal(ks[0], (N, DIN), dtype=jnp.float32)
        A = (jax.random.uniform(ks[1], (N, N)) < SPARSITY).astype(jnp.float32)
        left_weights = jax.random.normal(ks[2], (N, N), dtype=jnp.float32)

        def lin(k, fan_in, fan_out):
            k1, k2 = jax.random.split(k)
            bound = 1.0 / np.sqrt(fan_in)
            W = jax.random.uniform(k1, (fan_out, fan_in), minval=-bound, maxval=bound, dtype=jnp.float32)
            b = jax.random.uniform(k2, (fan_out,), minval=-bound, maxval=bound, dtype=jnp.float32)
            return (W, b)
        W0, b0 = lin(ks[3], DIN, DH)
        W1, b1 = lin(ks[4], DH, DH)
        W2, b2 = lin(ks[5], DH, DOUT)
        return {'x': x, 'A': A, 'left_weights': left_weights, 'W0': W0, 'b0': b0, 'W1': W1, 'b1': b1, 'W2': W2, 'b2': b2}
    _L1_gnn_all = _L1_gnn_setup()
    _L1_gnn_in = {k: v for k, v in _L1_gnn_all.items() if k in ('W0', 'b0', 'W1', 'b1', 'W2', 'b2')}
    del _L1_gnn_all

    def _L2_gnn_setup():
        import jax, jax.numpy as jnp
        import numpy as np
        N = 5000
        DIM = 64
        F_CONST = 1.0
        B_CONST = 0.1
        R_CONST = 0.01
        key = jax.random.key(seed)
        k1, k2 = jax.random.split(key)
        t = jnp.zeros((1,), dtype=jnp.float32)
        x = jax.random.uniform(k1, (N, DIM), dtype=jnp.float32)
        A = jax.random.uniform(k2, (N, N), dtype=jnp.float32)
        return {'t': t, 'x': x, 'A': A}
    _L2_gnn_all = _L2_gnn_setup()
    _L2_gnn_in = {k: v for k, v in _L2_gnn_all.items() if k in ('t',)}
    del _L2_gnn_all

    def _L3_gnn_setup():
        import jax, jax.numpy as jnp
        import numpy as np
        N = 8192
        F_IN = 64
        F_OUT = 64
        key = jax.random.key(seed)
        k1, k2, k3 = jax.random.split(key, 3)
        features = jax.random.normal(k1, (N, F_IN), dtype=jnp.float32)
        adj = jax.random.uniform(k2, (N, N), dtype=jnp.float32)
        W = jax.random.normal(k3, (F_OUT, 2 * F_IN), dtype=jnp.float32)
        return {'features': features, 'adj': adj, 'W': W}
    _L3_gnn_all = _L3_gnn_setup()
    _L3_gnn_in = {k: v for k, v in _L3_gnn_all.items() if k in ('W',)}
    del _L3_gnn_all
    return {'x': x, 'adj': adj, 'L0_gnn_W_u': _L0_gnn_in['W_u'], 'L0_gnn_diag_u': _L0_gnn_in['diag_u'], 'L0_gnn_par_u': _L0_gnn_in['par_u'], 'L0_gnn_W_i': _L0_gnn_in['W_i'], 'L0_gnn_diag_i': _L0_gnn_in['diag_i'], 'L0_gnn_par_i': _L0_gnn_in['par_i'], 'L0_gnn_ln_gamma': _L0_gnn_in['ln_gamma'], 'L0_gnn_ln_beta': _L0_gnn_in['ln_beta'], 'L1_gnn_W0': _L1_gnn_in['W0'], 'L1_gnn_b0': _L1_gnn_in['b0'], 'L1_gnn_W1': _L1_gnn_in['W1'], 'L1_gnn_b1': _L1_gnn_in['b1'], 'L1_gnn_W2': _L1_gnn_in['W2'], 'L1_gnn_b2': _L1_gnn_in['b2'], 'L2_gnn_t': _L2_gnn_in['t'], 'L3_gnn_W': _L3_gnn_in['W']}

def reference(x, adj, L0_gnn_W_u, L0_gnn_diag_u, L0_gnn_par_u, L0_gnn_W_i, L0_gnn_diag_i, L0_gnn_par_i, L0_gnn_ln_gamma, L0_gnn_ln_beta, L1_gnn_W0, L1_gnn_b0, L1_gnn_W1, L1_gnn_b1, L1_gnn_W2, L1_gnn_b2, L2_gnn_t, L3_gnn_W):
    import jax
    import jax.numpy as jnp

    def _L0_gnn_ref(ego_embeddings, adj, W_u, diag_u, par_u, W_i, diag_i, par_i, ln_gamma, ln_beta):
        import jax, jax.numpy as jnp
        import numpy as np
        N_USERS = 2048
        N_ITEMS = 3072
        EMB = 64
        LN_EPS = 1e-05
        nu = diag_u.shape[0]
        res = ego_embeddings
        ego_u = ego_embeddings[:nu]
        ego_i = ego_embeddings[nu:]
        u = par_u[0] * par_u[1] * (diag_u[:, None] * ego_u @ W_u) + ego_u
        i = par_i[0] * par_i[1] * (diag_i[:, None] * ego_i @ W_i) + ego_i
        e = jnp.concatenate([u, i], axis=0)
        h = adj @ (adj.T @ e)
        mu = jnp.mean(h, axis=-1, keepdims=True)
        var = jnp.var(h, axis=-1, keepdims=True)
        out = (h - mu) * jax.lax.rsqrt(var + LN_EPS) * ln_gamma + ln_beta + res
        return out

    def _L1_gnn_ref(x, A, left_weights, W0, b0, W1, b1, W2, b2):
        import jax, jax.numpy as jnp
        import numpy as np
        N = 4096
        DIN = 64
        DH = 64
        DOUT = 64
        SPARSITY = 0.01
        w = left_weights * A
        for W, b in ((W0, b0), (W1, b1), (W2, b2)):
            x = w @ x
            x = x @ W.T + b
        return x

    def _L2_gnn_ref(t, x, A):
        import jax, jax.numpy as jnp
        import numpy as np
        N = 5000
        DIM = 64
        F_CONST = 1.0
        B_CONST = 0.1
        R_CONST = 0.01
        Ax = A @ x
        outer = R_CONST * jnp.sum(x * Ax, axis=1, keepdims=True)
        return F_CONST - B_CONST * x - outer

    def _L3_gnn_ref(features, adj, W):
        import jax, jax.numpy as jnp
        import numpy as np
        N = 8192
        F_IN = 64
        F_OUT = 64
        neigh = jnp.matmul(adj, features)
        deg = jnp.sum(adj, axis=1, keepdims=True) + 1.0
        neigh = neigh / deg
        data = jnp.concatenate([features, neigh], axis=-1)
        return jnp.matmul(data, W.T)
    x = _layernorm(x + _L0_gnn_ref(x, adj, L0_gnn_W_u, L0_gnn_diag_u, L0_gnn_par_u, L0_gnn_W_i, L0_gnn_diag_i, L0_gnn_par_i, L0_gnn_ln_gamma, L0_gnn_ln_beta), axis=-1)
    x = _layernorm(x + _L1_gnn_ref(x, adj, adj, L1_gnn_W0, L1_gnn_b0, L1_gnn_W1, L1_gnn_b1, L1_gnn_W2, L1_gnn_b2), axis=-1)
    x = _layernorm(x + _L2_gnn_ref(L2_gnn_t, x, adj), axis=-1)
    x = _layernorm(x + _L3_gnn_ref(x, adj, L3_gnn_W), axis=-1)
    return x

_drawn_inputs = setup_inputs


def setup_inputs(seed=0):
    import zlib

    import numpy as np

    out = dict(_drawn_inputs(seed))
    spreads = {'L0_gnn_ln_gamma': (1.0, 0.2), 'L0_gnn_ln_beta': (0.0, 0.1)}
    factors = {'L0_gnn_diag_u': 64.0,
     'L0_gnn_W_i': 5.952,
     'L0_gnn_diag_i': 64.0,
     'L1_gnn_W0': 64.0,
     'L1_gnn_b0': 64.0,
     'L1_gnn_W1': 64.0,
     'L1_gnn_b1': 8.0,
     'L1_gnn_W2': 8.0}
    for name, (base, spread) in spreads.items():
        noise = np.random.default_rng([zlib.crc32(name.encode()), seed]).standard_normal(out[name].shape)
        drawn = base * np.exp(spread * noise) if base else spread * noise
        out[name] = jnp.asarray(drawn.astype(out[name].dtype))
    for name, factor in factors.items():
        out[name] = (out[name] * factor).astype(out[name].dtype)
    return out
```

```python
import concourse.bass as bass
from concourse import mybir
from contextlib import ExitStack

N = 5120
D = 64
P = 128
C = 512
NC = N // C
TC = C // P
NT = N // P
USERS = 2048
EPS = 1e-5
SLOTS = 8
BLOCK = TC * C

THIS, NEXT = 0, 1
SWEEPS = 7
ASC = {0: True, 1: True, 2: False, 3: True, 4: False, 5: True, 6: False}
MATRIX = {0: "A", 1: "A", 2: "W", 3: "W", 4: "W", 5: "A", 6: "A", 7: None}
LAG = {0: 0, 1: 2, 2: 3, 3: 3, 4: 2, 5: 3, 6: 0}

W_USER, W_ITEM, W_L1_0, W_L1_1, W_L1_2, W_SELF, W_NEIGH, W_EYE = range(8)
PROJECT = {0: W_EYE, 1: W_EYE, 2: W_L1_0, 3: W_L1_1, 4: W_L1_2, 5: W_EYE, 6: W_NEIGH}
V_GAMMA, V_BETA, V_B0, V_B1, V_B2 = range(5)
OPERAND = {0: 1, 1: 2, 2: 1, 3: 0, 4: 2, 5: 0, 6: 1, 7: 2}
RESIDUAL = {1: 0, 4: 1, 5: 0, 6: 1}


def plan():
    steps, bufs = [], []
    n = 0
    for s in range(SWEEPS):
        order = list(range(NC)) if ASC[s] else list(range(NC))[::-1]
        blocks = []
        for k, i in enumerate(order):
            done, ahead = order[:k], order[k + 1:]
            if s in (0, 1):
                js = [i] + ahead[::-1] + done
            elif s == 1:
                js = [i] + done
            else:
                js = [i] + done
            if s == 0:
                js = list(range(NC))
            for at, j in enumerate(js):
                blocks.append(dict(sweep=s, I=i, J=j, n=n + k, next=s not in (0, SWEEPS - 1) and j in done,
                                   first=at == 0, last=at == len(js) - 1,
                                   first_next=bool(done) and j == done[0],
                                   last_next=bool(done) and j == done[-1]))
        n += NC

        def load(b):
            if s > 0 and b["I"] == b["J"]:
                return None
            bufs.append(dict(kind="load", s=s, I=b["I"], J=b["J"], last=None))
            return len(bufs) - 1

        def square(of, b, in_place):
            if in_place:
                bufs[of]["squared"] = True
                return of
            bufs.append(dict(kind="square", of=of, I=b["I"], last=None))
            return len(bufs) - 1

        def step(b, part, buf, squared):
            steps.append(dict(sweep=s, I=b["I"], J=b["J"], part=part, buf=buf, squared=squared, n=b["n"],
                              first=b["first_next"] if part else b["first"],
                              last=b["last_next"] if part else b["last"]))
            if buf is not None:
                bufs[buf]["last"] = len(steps) - 1
                of = bufs[buf].get("of")
                if of is not None:
                    bufs[of]["last"] = len(steps) - 1

        lag = []
        for at, b in enumerate(blocks):
            own = load(b)
            this_w, next_w = MATRIX[s] == "W", MATRIX[s + 1] == "W"
            if this_w:
                in_place = own is not None and next_w
                this = square(own, b, in_place)
            else:
                in_place, this = False, own
            step(b, THIS, this, this_w)
            if b["next"]:
                lag.append((at, b, own, next_w))
            if lag and at - lag[0][0] >= LAG[s]:
                _, lb, lbuf, lw = lag.pop(0)
                step(lb, NEXT, lbuf, lw)
        for _, lb, lbuf, lw in lag:
            step(lb, NEXT, lbuf, lw)
    for k, b in enumerate(bufs):
        b["slot"] = k % SLOTS
        b["loads"] = sum(1 for x in bufs[b["slot"]:k + 1:SLOTS] if x["kind"] == "load")
    return steps, bufs


def layers_kernel(nc, out, Anat, At, x, xT, weights, vecs, diag, par, eye):
    f32 = mybir.dt.float32
    ALU = mybir.AluOpType
    ACT = mybir.ActivationFunctionType
    AX = mybir.AxisListType

    steps, bufs = plan()
    n_chunks = SWEEPS * NC

    squares, square_of = [], {}
    for k, st in enumerate(steps):
        if st["squared"]:
            buf = st["buf"]
            if bufs[buf]["kind"] == "square":
                if buf not in square_of:
                    square_of[buf] = len(squares)
                    squares.append((bufs[buf]["of"], st["I"], buf, None))
            elif buf not in square_of:
                square_of[buf] = len(squares)
                before = [q for q in range(k) if steps[q]["buf"] == buf]
                squares.append((buf, None, buf, before[-1] if before else None))

    chunk_end = {st["n"]: k for k, st in enumerate(steps) if st["last"] and st["part"] == THIS}
    next_end = {(st["sweep"], st["I"]): k for k, st in enumerate(steps) if st["last"] and st["part"] == NEXT}

    def result_of(sweep, i):
        return sweep * NC + (i if ASC[sweep] else NC - 1 - i)

    def needs(st):
        return result_of(st["sweep"] - 1 + st["part"], st["J"]) if st["sweep"] - 1 + st["part"] >= 0 else -1

    project_after = {}
    for n in range(n_chunks):
        k = chunk_end[n]
        nxt = k + 1
        if nxt < len(steps) and needs(steps[nxt]) != n:
            k = nxt
        project_after.setdefault(k, []).append(n)

    next_number = {key: q for q, (key, _) in enumerate(sorted(next_end.items(), key=lambda kv: kv[1]))}

    ctx = ExitStack()
    with ctx:
        def sb(name, shape):
            return ctx.enter_context(nc.sbuf_tensor(name, shape, f32))

        def ps(name, shape):
            return ctx.enter_context(nc.psum_tensor(name, shape, f32))

        def sem(name):
            return ctx.enter_context(nc.semaphore(name))

        slot_sb = [sb(f"slot{q}", [P, TC, C]) for q in range(SLOTS)]
        diag_sb = [sb(f"diagonal{i}", [P, TC, C]) for i in range(NC)]
        feat = [sb(f"features{q}", [P, NT, D]) for q in range(3)]
        partial = sb("partial", [P, NC, C])
        acc_sb = [sb(f"acc_sb{q}", [P, C]) for q in range(2)]
        w_sb = sb("weights_sb", [P, 8, D])
        v_sb = sb("vectors_sb", [P, 5, D])
        dg_sb = sb("row_scale", [P, NT])
        par_sb = sb("par_sb", [P, 4])
        pp_sb = sb("par_product", [P, 2])
        eye_sb = sb("eye_sb", [P, P])
        rowsum = sb("rowsum", [P, NC, NT])
        rdeg = sb("rdeg", [P, NT])
        h0 = sb("work0", [P, TC, D])
        h1 = sb("work1", [P, TC, D])
        h2 = sb("work2", [P, TC, D])
        s4 = sb("row_sum", [P, TC])
        v4 = sb("row_square_sum", [P, TC])
        r4 = sb("row_rstd", [P, TC])
        minus_half = sb("minus_half", [P, TC])
        xT_sb = partial[0:D, :, :].rearrange("p c n -> p (c n)")
        x3T = [feat[0][0:D, q * C // D:(q + 1) * C // D, :].rearrange("p t d -> p (t d)") for q in range(2)]

        acc = [ps(f"acc{q}", [P, C]) for q in range(2)]
        acc_next = [ps(f"acc_next{q}", [P, C]) for q in range(2)]
        nat = [ps(f"nat{q}", [P, 2, TC, D]) for q in range(2)]
        tr = ps("x3_transposed", [D, C])

        slot_loaded = [sem(f"slot{q}_loaded") for q in range(SLOTS)]
        diag_loaded = [sem(f"diagonal{i}_loaded") for i in range(NC)]
        inputs_loaded = sem("inputs_loaded")
        xT_loaded = sem("xT_loaded")
        steps_done = sem("steps_done")
        squares_done = sem("squares_done")
        rowsums_done = sem("rowsums_done")
        dense_done = sem("dense_done")
        e_ready = sem("e_ready")
        acc_copied = sem("acc_copied")
        partial_saved = sem("partial_saved")
        projected = sem("projected")
        x_ready = sem("x_ready")
        var_ready = sem("var_ready")
        rstd_ready = sem("rstd_ready")
        exponent_ready = sem("exponent_ready")
        x3_transposed = sem("x3_transposed")
        x3T_copied = sem("x3T_copied")
        dve_step = sem("dve_step")
        out_stored = sem("out_stored")
        N_INPUTS = 8

        def bcast4(ap):
            return ap.unsqueeze(2).to_broadcast([P, TC, D])

        def vec4(v):
            return v_sb[:, v, :].unsqueeze(1).to_broadcast([P, TC, D])

        block = ctx.enter_context(nc.Block())

        @block.sync
        def _(sp):
            sp.dma_start(xT_sb, xT).then_inc(xT_loaded, 16)
            sp.dma_start(w_sb[0:D], weights).then_inc(inputs_loaded, 16)
            sp.dma_start(w_sb[D:P], weights).then_inc(inputs_loaded, 16)
            sp.dma_start(v_sb[:], vecs).then_inc(inputs_loaded, 16)
            sp.dma_start(dg_sb[:], diag).then_inc(inputs_loaded, 16)
            sp.dma_start(par_sb[:], par).then_inc(inputs_loaded, 16)
            sp.dma_start(eye_sb[:], eye).then_inc(inputs_loaded, 16)
            sp.dma_start(feat[0][:], x).then_inc(inputs_loaded, 16)
            sp.dma_start(feat[1][:], x).then_inc(inputs_loaded, 16)
            for k, b in enumerate(bufs):
                if b["kind"] != "load":
                    continue
                if k >= SLOTS:
                    sp.wait_ge(steps_done, bufs[k - SLOTS]["last"] + 1)
                    if bufs[k - SLOTS].get("s") == 0:
                        sp.wait_ge(rowsums_done, k - SLOTS + 1)
                source = Anat if b["s"] == 0 else At
                sp.dma_start(slot_sb[b["slot"]][:], source[b["I"], b["J"]]).then_inc(slot_loaded[b["slot"]], 16)
                if k >= SLOTS - 1 and k < SLOTS - 1 + NC:
                    i = k - SLOTS + 1
                    sp.dma_start(diag_sb[i][:], At[i, i]).then_inc(diag_loaded[i], 16)

        @block.scalar
        def _(act):
            for src, diag_i, dst, before in squares:
                if src is None:
                    act.wait_ge(diag_loaded[diag_i], 16)
                    source = diag_sb[diag_i]
                else:
                    act.wait_ge(slot_loaded[bufs[src]["slot"]], 16 * bufs[src]["loads"])
                    source = slot_sb[bufs[src]["slot"]]
                if before is not None:
                    act.wait_ge(steps_done, before + 1)
                if dst != src and dst >= SLOTS:
                    act.wait_ge(steps_done, bufs[dst - SLOTS]["last"] + 1)
                nc.scalar.activation(slot_sb[bufs[dst]["slot"]][:], source[:], ACT.Square).then_inc(squares_done, 1)
            for k in range(NC):
                i = NC - 1 - k
                act.wait_ge(x_ready, (SWEEPS - 1) * NC + k + 1)
                act.dma_start(out[:, i * TC:(i + 1) * TC, :], feat[OPERAND[SWEEPS]][:, i * TC:(i + 1) * TC, :]).then_inc(out_stored, 16)
            act.wait_ge(out_stored, 16 * NC)

        @block.gpsimd
        def _(pool):
            nc.gpsimd.memset(minus_half[:], -0.5).then_inc(exponent_ready, 1)
            pool.wait_ge(exponent_ready, 1)
            for k in range(5 * NC):
                pool.wait_ge(var_ready, k + 1)
                nc.gpsimd.tensor_tensor(r4[:], v4[:], minus_half[:], ALU.pow).then_inc(rstd_ready, 1)

        @block.tensor
        def _(pe):
            pe.wait_ge(xT_loaded, 16)
            pe.wait_ge(inputs_loaded, 16 * N_INPUTS)
            banks = [acc[0], acc[1], acc_next[0], acc_next[1], tr]
            for g in range(NT // 8):
                for q in range(8):
                    t = 8 * g + q
                    w = W_USER if t < USERS // P else W_ITEM
                    bank = banks[g] if g < 4 else nat[0][:].rearrange("p a t d -> p (a t d)")
                    last = nc.tensor.matmul(bank[:, q * D:(q + 1) * D], xT_sb[:, t * P:(t + 1) * P],
                                            w_sb[0:D, w, :], start=True, stop=True)
                last.then_inc(dense_done, 1)

            pe.wait_ge(e_ready, NT // 8)
            known = 0
            for k, st in enumerate(steps):
                s, n, part = st["sweep"], st["n"], st["part"]
                if needs(st) + 1 > known:
                    known = needs(st) + 1
                    pe.wait_ge(x_ready, known)
                if st["buf"] is None:
                    pe.wait_ge(diag_loaded[st["I"]], 16)
                    a = diag_sb[st["I"]]
                else:
                    b = bufs[st["buf"]]
                    a = slot_sb[b["slot"]]
                    if st["squared"]:
                        pe.wait_ge(squares_done, square_of[st["buf"]] + 1)
                    else:
                        pe.wait_ge(slot_loaded[b["slot"]], 16 * b["loads"])
                if part == THIS:
                    bank = acc[n % 2]
                    if st["first"] and n >= 2:
                        pe.wait_ge(acc_copied, n - 1)
                else:
                    m = next_number[(s, st["I"])]
                    bank = acc_next[m % 2]
                    if st["first"] and m >= 2:
                        pe.wait_ge(partial_saved, m - 1)
                x_op = feat[OPERAND[s + part]]
                for q in range(TC):
                    half = slice(D * (q % 2), D * (q % 2) + D)
                    last = nc.tensor.matmul(bank[half, :], x_op[:, st["J"] * TC + q, :], a[:, q, :],
                                            start=st["first"] and q < 2, stop=st["last"] and q >= 2)
                last.then_inc(steps_done, 1)

                if s == SWEEPS - 1 and st["first"]:
                    if n > (SWEEPS - 1) * NC:
                        pe.wait_ge(x3T_copied, n - (SWEEPS - 1) * NC)
                    for q in range(TC):
                        last = nc.tensor.transpose(tr[:, q * P:(q + 1) * P], feat[OPERAND[s]][:, st["I"] * TC + q, :], eye_sb[:])
                    last.then_inc(x3_transposed, 1)

                for m in project_after.get(k, []):
                    ms = m // NC
                    pe.wait_ge(acc_copied, m + 1)
                    if m >= 2:
                        pe.wait_ge(x_ready, m - 1)
                    for q in range(TC):
                        last = nc.tensor.matmul(nat[m % 2][:, 0, q, :], acc_sb[m % 2][:, q * P:(q + 1) * P],
                                                w_sb[:, PROJECT[ms], :], start=True, stop=True)
                    if ms == SWEEPS - 1:
                        mc = m - (SWEEPS - 1) * NC
                        pe.wait_ge(x3T_copied, mc + 1)
                        for q in range(TC):
                            last = nc.tensor.matmul(nat[m % 2][:, 1, q, :], x3T[mc % 2][:, q * P:(q + 1) * P],
                                                    w_sb[0:D, W_SELF, :], start=True, stop=True)
                    last.then_inc(projected, 1)

        @block.vector
        def _(dve):
            chain = [0]
            norms = [0]

            def link(ins):
                chain[0] += 1
                ins.then_inc(dve_step, 1)
                dve.wait_ge(dve_step, chain[0])

            V = nc.vector

            def centre(src):
                link(V.tensor_reduce(s4[:], src, AX.X, ALU.add))
                link(V.scalar_tensor_tensor(h1[:], bcast4(s4[:]), -1.0 / D, src, ALU.mult, ALU.add))
                link(V.tensor_tensor(h2[:], h1[:], h1[:], ALU.mult))
                norms[0] += 1
                link(V.tensor_reduce(s4[:], h2[:], AX.X, ALU.add))
                V.tensor_scalar(v4[:], s4[:], D * EPS, None, ALU.add).then_inc(var_ready, 1)
                dve.wait_ge(rstd_ready, norms[0])

            def normed(dst):
                return V.scalar_tensor_tensor(dst, h1[:], float(D) ** 0.5, bcast4(r4[:]), ALU.mult, ALU.mult)

            def finish(n):
                s = n // NC
                i = (n % NC) if ASC[s] else NC - 1 - n % NC
                rows = slice(i * TC, (i + 1) * TC)
                src = nat[n % 2][:, 0]
                dst = feat[OPERAND[s + 1]][:, rows, :]
                dve.wait_ge(projected, n + 1)
                if s == 0:
                    last = V.tensor_copy(dst, src)
                elif s == 1:
                    centre(src)
                    link(normed(h0[:]))
                    link(V.tensor_tensor(h0[:], h0[:], vec4(V_GAMMA), ALU.mult))
                    link(V.tensor_tensor(h0[:], h0[:], vec4(V_BETA), ALU.add))
                    link(V.scalar_tensor_tensor(h0[:], feat[RESIDUAL[s]][:, rows, :], 2.0, h0[:], ALU.mult, ALU.add))
                    centre(h0[:])
                    last = normed(dst)
                elif s in (2, 3):
                    last = V.tensor_tensor(dst, src, vec4(V_B0 + s - 2), ALU.add)
                elif s == 4:
                    link(V.tensor_tensor(h0[:], src, vec4(V_B2), ALU.add))
                    link(V.tensor_tensor(h0[:], h0[:], feat[RESIDUAL[s]][:, rows, :], ALU.add))
                    centre(h0[:])
                    last = normed(dst)
                elif s == 5:
                    x2 = feat[RESIDUAL[s]][:, rows, :]
                    link(V.tensor_tensor(h0[:], src, x2, ALU.mult))
                    link(V.tensor_reduce(s4[:], h0[:], AX.X, ALU.add))
                    link(V.tensor_scalar(h2[:], x2, 0.9, 1.0, ALU.mult, ALU.add))
                    link(V.scalar_tensor_tensor(h0[:], bcast4(s4[:]), -0.01, h2[:], ALU.mult, ALU.add))
                    centre(h0[:])
                    last = normed(dst)
                else:
                    link(V.tensor_tensor(h0[:], src, bcast4(rdeg[:, rows]), ALU.mult))
                    link(V.tensor_tensor(h0[:], h0[:], nat[n % 2][:, 1], ALU.add))
                    link(V.tensor_tensor(h0[:], h0[:], feat[RESIDUAL[s]][:, rows, :], ALU.add))
                    centre(h0[:])
                    last = normed(dst)
                last.then_inc(x_ready, 1)
                dve.wait_ge(x_ready, n + 1)

            dve.wait_ge(inputs_loaded, 16 * N_INPUTS)
            link(V.tensor_tensor(pp_sb[:], par_sb[:, 0:4:2], par_sb[:, 1:4:2], ALU.mult))
            UT = USERS // P
            link(V.tensor_scalar(dg_sb[:, 0:UT], dg_sb[:, 0:UT], pp_sb[:, 0:1], None, ALU.mult))
            link(V.tensor_scalar(dg_sb[:, UT:NT], dg_sb[:, UT:NT], pp_sb[:, 1:2], None, ALU.mult))
            for g in range(NT // 8):
                rows = slice(8 * g, 8 * g + 8)
                bank = [acc[0][:], acc[1][:], acc_next[0][:], acc_next[1][:],
                        nat[0][:].rearrange("p a t d -> p (a t d)")][g].rearrange("p (t d) -> p t d", d=D)
                dve.wait_ge(dense_done, g + 1)
                e_part = slot_free = rowsum[:, :, :]
                link(V.tensor_tensor(bank, bank, dg_sb[:, rows].unsqueeze(2).to_broadcast([P, 8, D]), ALU.mult))
                V.tensor_tensor(feat[1][:, rows, :], bank, feat[0][:, rows, :], ALU.add).then_inc(e_ready, 1)
            dve.wait_ge(e_ready, NT // 8)

            for k, st in enumerate(steps):
                s, n = st["sweep"], st["n"]
                if s == 0:
                    b = bufs[st["buf"]]
                    dve.wait_ge(slot_loaded[b["slot"]], 16 * b["loads"])
                    V.tensor_reduce(rowsum[:, st["I"], st["J"] * TC:(st["J"] + 1) * TC], slot_sb[b["slot"]][:],
                                    AX.X, ALU.add).then_inc(rowsums_done, 1)
                if chunk_end.get(n) == k:
                    dve.wait_ge(steps_done, k + 1)
                    if n >= 2:
                        dve.wait_ge(projected, n - 1)
                    if (s - 1, st["I"]) in next_number:
                        dve.wait_ge(partial_saved, next_number[(s - 1, st["I"])] + 1)
                        V.tensor_tensor(acc_sb[n % 2][:], acc[n % 2][:], partial[:, st["I"], :], ALU.add).then_inc(acc_copied, 1)
                        dve.wait_ge(acc_copied, n + 1)
                    else:
                        V.tensor_copy(acc_sb[n % 2][:], acc[n % 2][:]).then_inc(acc_copied, 1)
                if next_end.get((s, st["I"])) == k:
                    m = next_number[(s, st["I"])]
                    dve.wait_ge(steps_done, k + 1)
                    V.tensor_copy(partial[:, st["I"], :], acc_next[m % 2][:]).then_inc(partial_saved, 1)
                if s == SWEEPS - 1 and st["first"]:
                    c = n - (SWEEPS - 1) * NC
                    dve.wait_ge(x3_transposed, c + 1)
                    if c >= 2:
                        dve.wait_ge(projected, n - 1)
                    V.tensor_copy(x3T[c % 2], tr[:]).then_inc(x3T_copied, 1)
                for m in project_after.get(k, []):
                    finish(m)
                if s == 1 and k == chunk_end[NC] :
                    dve.wait_ge(rowsums_done, NC * NC)
                    link(V.tensor_reduce(rdeg[:], rowsum[:].rearrange("p c t -> p t c"), AX.X, ALU.add))
                    link(V.tensor_scalar(rdeg[:], rdeg[:], 1.0, None, ALU.add))
                    link(V.reciprocal(rdeg[:], rdeg[:]))


def kernel(**inputs):
    import numpy as np
    import concourse.bacc as bacc
    from concourse.bass_utils import run_bass_kernel_spmd

    a = {k: np.asarray(v) for k, v in inputs.items()}
    A = a["adj"]

    def blocks(m):
        return np.ascontiguousarray(m.reshape(NC, TC, P, NC, C).transpose(3, 0, 2, 1, 4))

    def tiled(v):
        return np.ascontiguousarray(np.moveaxis(v.reshape(NT, P, *v.shape[1:]), 0, 1))

    L3 = a["L3_gnn_W"]
    weights = np.ascontiguousarray(np.stack([
        a["L0_gnn_W_u"], a["L0_gnn_W_i"], a["L1_gnn_W0"].T, a["L1_gnn_W1"].T, a["L1_gnn_W2"].T,
        L3[:, :D].T, L3[:, D:].T, np.eye(D, dtype=np.float32)], axis=1))
    vecs = np.ascontiguousarray(np.broadcast_to(np.stack([
        a["L0_gnn_ln_gamma"], a["L0_gnn_ln_beta"], a["L1_gnn_b0"], a["L1_gnn_b1"], a["L1_gnn_b2"]]), (P, 5, D)))
    par = np.ascontiguousarray(np.broadcast_to(np.concatenate([a["L0_gnn_par_u"], a["L0_gnn_par_i"]]), (P, 4)))
    arrays = {
        "A_natural": blocks(A), "A_transposed": blocks(A.T),
        "x": tiled(a["x"]), "xT": np.ascontiguousarray(a["x"].T), "weights": weights, "vecs": vecs,
        "diag": tiled(np.concatenate([a["L0_gnn_diag_u"], a["L0_gnn_diag_i"]])), "par": par,
        "eye": np.eye(P, dtype=np.float32),
    }
    nc = bacc.Bacc("TRN2", target_bir_lowering=False, num_devices=1)
    args = [nc.dram_tensor(f"in_{k}", v.shape, mybir.dt.float32, kind="ExternalInput").ap() for k, v in arrays.items()]
    out = nc.dram_tensor("out", (P, NT, D), mybir.dt.float32, kind="ExternalOutput").ap()
    layers_kernel(nc, out, *args)
    r = run_bass_kernel_spmd(nc, [{f"in_{k}": v for k, v in arrays.items()}], core_ids=[0])
    got = r.results[0]["out"]
    return np.ascontiguousarray(np.moveaxis(got, 0, 1)).reshape(N, D)
```

```python
import concourse.bass as bass
from concourse import mybir
from contextlib import ExitStack

N = 5120
D = 64
P = 128
C = 512
NC = N // C
TC = C // P
NT = N // P
USERS = 2048
EPS = 1e-5
SLOTS = 8
BLOCK = TC * C

THIS, NEXT, BOTH, TURN = 0, 1, 2, 3
SWEEPS = 7
ASC = {0: True, 1: True, 2: False, 3: True, 4: False, 5: True, 6: True}
MATRIX = {0: "A", 1: "A", 2: "W", 3: "W", 4: "W", 5: "A", 6: "A", 7: None}
LAG = {1: 2, 2: 3, 3: 3, 4: 2, 5: 3, 6: 0}
LAG_SQUARE = 2
SETTLED = 4
EARLY = (6, 7, 8, 9)
EARLY_LOADS = {(1, 6): 9, (2, 1): 8, (2, 5): 7, (3, 1): 6}
KEPT_LOADS = {(0, 3): 0, (0, 4): 1, (0, 6): 2, (1, 1): 3, (1, 4): 4, (2, 3): 5, (3, 3): 6, (4, 3): 7, (5, 3): 8, (6, 3): 9}

W_USER, W_ITEM, W_L1_0, W_L1_1, W_L1_2, W_SELF, W_NEIGH, W_EYE = range(8)
PROJECT = {0: W_EYE, 1: W_EYE, 2: W_L1_0, 3: W_L1_1, 4: W_L1_2, 5: W_EYE, 6: W_NEIGH}
V_GAMMA, V_BETA, V_B0, V_B1, V_B2 = range(5)
OPERAND = {0: 0, 1: 2, 2: 0, 3: 1, 4: 2, 5: 1, 6: 0, 7: 2}
RESIDUAL = {1: 1, 4: 0, 5: 1, 6: 0}
X_BUF = 1


def blocks_of(s):
    order = list(range(NC)) if ASC[s] else list(range(NC))[::-1]
    for k, i in enumerate(order):
        done, ahead = order[:k], order[k + 1:]
        if s == 0:
            js = list(range(NC))
        elif s == 1:
            js = [i] + ahead[::-1] + done
        elif s < SWEEPS - 1:
            js = [i] + done
        else:
            js = [i] + ahead
        yield k, i, js, done if 0 < s < SWEEPS - 1 else []


def plan():
    steps, bufs, issue, turns = [], [], [], []

    def add(s, k, i, j, part, source, buf=None, turn=None, squared=False):
        steps.append(dict(sweep=s, I=i, J=j, part=part, n=s * NC + k, source=source, buf=buf, turn=turn,
                          squared=squared))
        q = len(steps) - 1
        if buf is not None:
            bufs[buf]["last"] = q
            bufs[buf].setdefault("use", q)
            of = bufs[buf].get("of")
            if of is not None:
                bufs[of]["last"] = max(bufs[of].get("last", 0), q)

    def load(s, i, j):
        bufs.append(dict(kind="load", s=s, I=i, J=j))
        issue.append(("slot", len(bufs) - 1))
        return len(bufs) - 1

    early = {}
    for k, i, js, _ in blocks_of(0):
        turned = [i] + ([0] if i in EARLY else [])
        natural = [j for j in js if j not in turned]
        waiting = []
        for at, j in enumerate(natural):
            buf = load(0, i, j)
            if (k, at) in KEPT_LOADS:
                issue.append(("kept", KEPT_LOADS[k, at]))
            if (k, at) in EARLY_LOADS:
                col = EARLY_LOADS[k, at]
                early[col] = load(1, 0, col)
            add(0, k, i, j, THIS, "slot", buf)
            if at in (1, 4) and turned:
                j = turned.pop(0)
                turns.append(dict(I=j, J=i, buf=None if j == i else early[i]))
                turn = len(turns) - 1
                turns[turn]["step"] = len(steps)
                add(0, k, i, j, TURN, "kept" if j == i else "slot", turns[turn]["buf"], turn)
                waiting.append((at + 2, j, turn))
            if waiting and waiting[0][0] == at:
                _, j, turn = waiting.pop(0)
                add(0, k, i, j, THIS, "turned", turn=turn)

    for s in range(1, SWEEPS):
        this_w, next_w = MATRIX[s] == "W", MATRIX[s + 1] == "W"
        lag, at = [], 0

        def due():
            while lag and at >= lag[0][0]:
                lag.pop(0)[1]()

        for k, i, js, shared in blocks_of(s):
            for j in js:
                kept = i == j
                if s == 1 and i == 0 and j in early:
                    own = early[j]
                else:
                    own = None if kept else load(s, i, j)
                here = "kept" if kept else "slot"
                both = j in shared and this_w == next_w and k >= SETTLED
                next_first = j in shared and this_w and not next_w and k >= SETTLED
                if both:
                    add(s, k, i, j, BOTH, here, own, squared=this_w)
                elif next_first:
                    add(s, k, i, j, NEXT, here, own)
                    lag.append((at + LAG_SQUARE, lambda k=k, i=i, j=j, own=own: add(s, k, i, j, THIS, "slot", own, squared=True)))
                else:
                    this = own
                    if this_w and not (own is not None and next_w):
                        bufs.append(dict(kind="square", of=own, I=i))
                        this = len(bufs) - 1
                    if k >= SETTLED and this_w and not next_w:
                        lag.append((at + LAG_SQUARE, lambda k=k, i=i, j=j, this=this: add(s, k, i, j, THIS, "slot", this, squared=True)))
                    else:
                        add(s, k, i, j, THIS, "slot" if this is not None else here, this, squared=this_w)
                    if j in shared:
                        lag.append((at + LAG[s], lambda k=k, i=i, j=j, own=own: add(s, k, i, j, NEXT, "slot", own, squared=next_w)))
                due()
                at += 1
        at += NC * NC
        due()

    ends = {}
    for q, st in enumerate(steps):
        if st["part"] != TURN:
            for part in ((THIS, NEXT) if st["part"] == BOTH else (st["part"],)):
                ends.setdefault((st["n"], part), [q, q])[1] = q

    held = [None] * SLOTS
    loads = [0] * SLOTS
    for k, b in enumerate(bufs):
        slot = min(range(SLOTS), key=lambda q: -1 if held[q] is None else bufs[held[q]]["last"])
        b["slot"], b["before"] = slot, held[slot]
        assert b["before"] is None or bufs[b["before"]]["last"] < b["use"]
        held[slot] = k
        loads[slot] += b["kind"] == "load"
        b["loads"] = loads[slot]
    return steps, bufs, issue, turns, ends


def layers_kernel(nc, out, Anat, At, x, weights, vecs, diag, par, eye):
    f32 = mybir.dt.float32
    ALU = mybir.AluOpType
    ACT = mybir.ActivationFunctionType
    AX = mybir.AxisListType

    steps, bufs, issue, turns, ends = plan()
    n_chunks = SWEEPS * NC

    squares, square_of = [], {}
    for k, st in enumerate(steps):
        buf = st["buf"]
        if st["squared"] and buf not in square_of:
            square_of[buf] = len(squares)
            if bufs[buf]["kind"] == "square":
                squares.append((bufs[buf]["of"], st["I"], buf, None))
            else:
                before = [q for q in range(k) if steps[q]["buf"] == buf]
                squares.append((buf, None, buf, before[-1] if before else None))

    def row_chunk(n):
        return n % NC if ASC[n // NC] else NC - 1 - n % NC

    def result_of(s, i):
        return s * NC + (i if ASC[s] else NC - 1 - i)

    def needs(st):
        if st["part"] == TURN:
            return -1
        s = st["sweep"] - (st["part"] == THIS)
        return result_of(s, st["J"]) if s >= 0 else -1

    project_after = {}
    for n in range(n_chunks):
        k = ends[n, THIS][1]
        if k + 1 < len(steps) and needs(steps[k + 1]) != n:
            k += 1
        project_after.setdefault(k, []).append(n)
    this_end = {ends[n, THIS][1]: n for n in range(n_chunks)}
    next_end = {q[1]: n for (n, part), q in ends.items() if part == NEXT}
    next_number = {n: m for m, (_, n) in enumerate(sorted(next_end.items()))}
    save_after = {max(k, ends[n, THIS][1]): n for k, n in next_end.items()}
    both_chunk = {st["n"] for st in steps if st["part"] == BOTH}
    rowsum_number = {k: q for q, k in enumerate(k for k, st in enumerate(steps) if st["sweep"] == 0 and st["part"] == THIS)}
    rowsum_of_buf = {steps[k]["buf"]: q for k, q in rowsum_number.items() if steps[k]["source"] == "slot"}
    turned_use = {steps[k]["turn"]: (k, q) for k, q in rowsum_number.items() if steps[k]["source"] == "turned"}

    def halves(s):
        t, x = OPERAND[s], OPERAND[s + 1]
        low, high = slice(0, D), slice(D, P)
        assert abs(t - x) == 1
        return (t, low, high) if t < x else (x, high, low)

    ctx = ExitStack()
    with ctx:
        def sb(name, shape):
            return ctx.enter_context(nc.sbuf_tensor(name, shape, f32))

        def ps(name, shape):
            return ctx.enter_context(nc.psum_tensor(name, shape, f32))

        def sem(name):
            return ctx.enter_context(nc.semaphore(name))

        slot_sb = [sb(f"slot{q}", [P, TC, C]) for q in range(SLOTS)]
        diag_sb = [sb(f"diagonal{i}", [P, TC, C]) for i in range(NC)]
        feats = sb("features", [P, NT, 3, D])
        feat = [feats[:, :, q, :] for q in range(3)]
        partial = sb("partial", [P, NC, C])
        acc_sb = [sb(f"acc_sb{q}", [P, C]) for q in range(2)]
        w_sb = sb("weights_sb", [P, 8, D])
        v_sb = sb("vectors_sb", [P, 5, D])
        dg_sb = sb("row_scale", [P, NT])
        par_sb = sb("par_sb", [P, 4])
        pp_sb = sb("par_product", [P, 2])
        eye_sb = sb("eye_sb", [P, P])
        spare = sb("rowsums_then_x3T", [P, C])
        rowsum = spare[:, 0:NC * NT].rearrange("p (c t) -> p c t", c=NC)
        rdeg = sb("rdeg", [P, NT])
        h0 = sb("work0", [P, TC, D])
        h1 = sb("work1", [P, TC, D])
        h2 = sb("work2", [P, TC, D])
        s4 = sb("row_sum", [P, TC])
        v4 = sb("row_square_sum", [P, TC])
        r4 = sb("row_rstd", [P, TC])
        minus_half = sb("minus_half", [P, TC])
        xT_sb = partial[0:D, :, :].rearrange("p c n -> p (c n)")
        turned_sb = [partial[:, q * TC:(q + 1) * TC, :] for q in range(2)]
        x3T = spare[0:D, :]

        acc = [ps(f"acc{q}", [P, C]) for q in range(2)]
        acc_next = [ps(f"acc_next{q}", [P, C]) for q in range(2)]
        nat = [ps(f"nat{q}", [P, 2, TC, D]) for q in range(2)]
        tr = [ps(f"transposed{q}", [P, C]) for q in range(2)]
        turn_banks = [acc_next[0], acc_next[1], tr[0], tr[1]]

        slot_loaded = [sem(f"slot{q}_loaded") for q in range(SLOTS)]
        diag_loaded = [sem(f"diagonal{i}_loaded") for i in range(NC)]
        inputs_loaded = sem("inputs_loaded")
        x_loaded = sem("x_loaded")
        x_transposed = sem("x_transposed")
        xT_copied = sem("xT_copied")
        steps_done = sem("steps_done")
        squares_done = sem("squares_done")
        rowsums_done = sem("rowsums_done")
        dense_done = sem("dense_done")
        e_ready = sem("e_ready")
        acc_copied = sem("acc_copied")
        partial_saved = sem("partial_saved")
        projected = sem("projected")
        x_ready = sem("x_ready")
        var_ready = sem("var_ready")
        rstd_ready = sem("rstd_ready")
        exponent_ready = sem("exponent_ready")
        turn_row_done = sem("turn_row_done")
        turn_row_copied = sem("turn_row_copied")
        x3_transposed = sem("x3_transposed")
        x3T_copied = sem("x3T_copied")
        dve_step = sem("dve_step")
        out_stored = sem("out_stored")
        N_INPUTS = 6

        def bcast4(ap):
            return ap.unsqueeze(2).to_broadcast([P, TC, D])

        def vec4(v):
            return v_sb[:, v, :].unsqueeze(1).to_broadcast([P, TC, D])

        dense_banks = [acc[0][:], acc[1][:], nat[0][:].rearrange("p a t d -> p (a t d)"),
                       nat[1][:].rearrange("p a t d -> p (a t d)"), acc_next[0][:]]

        block = ctx.enter_context(nc.Block())

        @block.sync
        def _(sp):
            sp.dma_start(feat[X_BUF], x).then_inc(x_loaded, 16)
            sp.dma_start(eye_sb[:], eye).then_inc(inputs_loaded, 16)
            sp.dma_start(w_sb[0:D], weights).then_inc(inputs_loaded, 16)
            sp.dma_start(w_sb[D:P], weights).then_inc(inputs_loaded, 16)
            sp.dma_start(v_sb[:], vecs).then_inc(inputs_loaded, 16)
            sp.dma_start(dg_sb[:], diag).then_inc(inputs_loaded, 16)
            sp.dma_start(par_sb[:], par).then_inc(inputs_loaded, 16)
            for what, k in issue:
                if what == "kept":
                    sp.dma_start(diag_sb[k][:], At[k, k]).then_inc(diag_loaded[k], 16)
                    continue
                b = bufs[k]
                if b["before"] is not None:
                    sp.wait_ge(steps_done, bufs[b["before"]]["last"] + 1)
                    if b["before"] in rowsum_of_buf:
                        sp.wait_ge(rowsums_done, rowsum_of_buf[b["before"]] + 1)
                source = Anat if b["s"] == 0 else At
                sp.dma_start(slot_sb[b["slot"]][:], source[b["I"], b["J"]]).then_inc(slot_loaded[b["slot"]], 16)

        @block.scalar
        def _(act):
            for g in range(NT // 8):
                for h in range(2):
                    act.wait_ge(x_transposed, 2 * g + h + 1)
                    nc.scalar.copy(xT_sb[:, (2 * g + h) * C:(2 * g + h + 1) * C], turn_banks[(2 * g + h) % 4][0:D, :]).then_inc(xT_copied, 1)
            for t in range(len(turns)):
                if t >= 2:
                    act.wait_ge(steps_done, turned_use[t - 2][0] + 1)
                    act.wait_ge(rowsums_done, turned_use[t - 2][1] + 1)
                for r in range(TC):
                    if r < TC - 1:
                        act.wait_ge(turn_row_done, t * (TC - 1) + r + 1)
                    else:
                        act.wait_ge(steps_done, turns[t]["step"] + 1)
                    nc.scalar.copy(turned_sb[t % 2][:, r, :], turn_banks[r][:]).then_inc(turn_row_copied, 1)
            for src, diag_i, dst, before in squares:
                if src is None:
                    act.wait_ge(diag_loaded[diag_i], 16)
                    source = diag_sb[diag_i]
                else:
                    act.wait_ge(slot_loaded[bufs[src]["slot"]], 16 * bufs[src]["loads"])
                    source = slot_sb[bufs[src]["slot"]]
                if before is not None:
                    act.wait_ge(steps_done, before + 1)
                if dst != src:
                    act.wait_ge(steps_done, bufs[bufs[dst]["before"]]["last"] + 1)
                nc.scalar.activation(slot_sb[bufs[dst]["slot"]][:], source[:], ACT.Square).then_inc(squares_done, 1)
            for i in range(NC):
                act.wait_ge(x_ready, (SWEEPS - 1) * NC + i + 1)
                act.dma_start(out[:, i * TC:(i + 1) * TC, :], feat[OPERAND[SWEEPS]][:, i * TC:(i + 1) * TC, :]).then_inc(out_stored, 16)
            act.wait_ge(out_stored, 16 * NC)

        @block.gpsimd
        def _(pool):
            nc.gpsimd.memset(minus_half[:], -0.5).then_inc(exponent_ready, 1)
            pool.wait_ge(exponent_ready, 1)
            for k in range(5 * NC):
                pool.wait_ge(var_ready, k + 1)
                nc.gpsimd.tensor_tensor(r4[:], v4[:], minus_half[:], ALU.pow).then_inc(rstd_ready, 1)

        @block.tensor
        def _(pe):
            pe.wait_ge(inputs_loaded, 16 * N_INPUTS)
            pe.wait_ge(x_loaded, 16)
            for c in range(NC):
                if c >= 4:
                    pe.wait_ge(xT_copied, c - 3)
                for q in range(TC):
                    last = nc.tensor.transpose(turn_banks[c % 4][0:D, q * P:(q + 1) * P], feat[X_BUF][:, c * TC + q, :], eye_sb[:])
                last.then_inc(x_transposed, 1)
            for g in range(NT // 8):
                pe.wait_ge(xT_copied, 2 * g + 2)
                for q in range(8):
                    t = 8 * g + q
                    w = W_USER if t < USERS // P else W_ITEM
                    last = nc.tensor.matmul(dense_banks[g][:, q * D:(q + 1) * D], xT_sb[:, t * P:(t + 1) * P],
                                            w_sb[0:D, w, :], start=True, stop=True)
                last.then_inc(dense_done, 1)

            pe.wait_ge(e_ready, NT // 8)
            known = 0
            for k, st in enumerate(steps):
                s, n, part = st["sweep"], st["n"], st["part"]
                first = [p for p in (THIS, NEXT) if ends.get((n, p), (None,))[0] == k]
                if needs(st) + 1 > known:
                    known = needs(st) + 1
                    pe.wait_ge(x_ready, known)
                if st["source"] == "kept":
                    pe.wait_ge(diag_loaded[st["J"]], 16)
                    a = diag_sb[st["J"]]
                elif st["source"] == "turned":
                    pe.wait_ge(turn_row_copied, (st["turn"] + 1) * TC)
                    a = turned_sb[st["turn"] % 2]
                else:
                    b = bufs[st["buf"]]
                    a = slot_sb[b["slot"]]
                    if st["squared"]:
                        pe.wait_ge(squares_done, square_of[st["buf"]] + 1)
                    else:
                        pe.wait_ge(slot_loaded[b["slot"]], 16 * b["loads"])
                if part == TURN:
                    for r in range(TC):
                        if st["turn"] > 0:
                            pe.wait_ge(turn_row_copied, (st["turn"] - 1) * TC + r + 1)
                        for q in range(TC):
                            last = nc.tensor.transpose(turn_banks[r][:, q * P:(q + 1) * P], a[:, q, r * P:(r + 1) * P], eye_sb[:])
                        if r < TC - 1:
                            last.then_inc(turn_row_done, 1)
                if THIS in first and n >= 2:
                    pe.wait_ge(acc_copied, n - 1)
                if NEXT in first:
                    m = next_number[n]
                    if m >= 2:
                        pe.wait_ge(partial_saved, m - 1)
                if part == BOTH:
                    low, _, _ = halves(s)
                    bank = acc_next[next_number[n] % 2]
                    for q in range(TC):
                        last = nc.tensor.matmul(bank[:], feats[:, st["J"] * TC + q, low:low + 2, :].rearrange("p b d -> p (b d)"), a[:, q, :],
                                                start=NEXT in first and q == 0, stop=q == TC - 1 and next_end.get(k) == n)
                elif part in (THIS, NEXT):
                    bank = acc[n % 2] if part == THIS else acc_next[next_number[n] % 2]
                    x_op = feat[OPERAND[s + part]]
                    ends_here = (this_end if part == THIS else next_end).get(k) == n
                    if part == THIS and n in both_chunk:
                        ends_here = True
                    for q in range(TC):
                        half = slice(D * (q % 2), D * (q % 2) + D)
                        last = nc.tensor.matmul(bank[half, :], x_op[:, st["J"] * TC + q, :], a[:, q, :],
                                                start=part in first and q < 2, stop=ends_here and q >= 2)
                last.then_inc(steps_done, 1)

                if s == SWEEPS - 1 and THIS in first:
                    if n > (SWEEPS - 1) * NC:
                        pe.wait_ge(x3T_copied, n - (SWEEPS - 1) * NC)
                    for q in range(TC):
                        last = nc.tensor.transpose(tr[0][0:D, q * P:(q + 1) * P], feat[OPERAND[s]][:, st["I"] * TC + q, :], eye_sb[:])
                    last.then_inc(x3_transposed, 1)

                for m in project_after.get(k, []):
                    ms = m // NC
                    pe.wait_ge(acc_copied, m + 1)
                    if m >= 2:
                        pe.wait_ge(x_ready, m - 1)
                    for q in range(TC):
                        last = nc.tensor.matmul(nat[m % 2][:, 0, q, :], acc_sb[m % 2][:, q * P:(q + 1) * P],
                                                w_sb[:, PROJECT[ms], :], start=True, stop=True)
                    if ms == SWEEPS - 1:
                        mc = m - (SWEEPS - 1) * NC
                        pe.wait_ge(x3T_copied, mc + 1)
                        for q in range(TC):
                            last = nc.tensor.matmul(nat[m % 2][:, 1, q, :], x3T[:, q * P:(q + 1) * P],
                                                    w_sb[0:D, W_SELF, :], start=True, stop=True)
                    last.then_inc(projected, 1)

        @block.vector
        def _(dve):
            chain = [0]
            norms = [0]

            def link(ins):
                chain[0] += 1
                ins.then_inc(dve_step, 1)
                dve.wait_ge(dve_step, chain[0])

            V = nc.vector

            def centre(src):
                link(V.tensor_reduce(s4[:], src, AX.X, ALU.add))
                link(V.scalar_tensor_tensor(h1[:], bcast4(s4[:]), -1.0 / D, src, ALU.mult, ALU.add))
                link(V.tensor_tensor(h2[:], h1[:], h1[:], ALU.mult))
                norms[0] += 1
                link(V.tensor_reduce(s4[:], h2[:], AX.X, ALU.add))
                V.tensor_scalar(v4[:], s4[:], D * EPS, None, ALU.add).then_inc(var_ready, 1)
                dve.wait_ge(rstd_ready, norms[0])

            def normed(dst):
                return V.scalar_tensor_tensor(dst, h1[:], float(D) ** 0.5, bcast4(r4[:]), ALU.mult, ALU.mult)

            def finish(n):
                s = n // NC
                i = row_chunk(n)
                rows = slice(i * TC, (i + 1) * TC)
                src = nat[n % 2][:, 0]
                dst = feat[OPERAND[s + 1]][:, rows, :]
                dve.wait_ge(projected, n + 1)
                if s == 0:
                    last = V.tensor_copy(dst, src)
                elif s == 1:
                    centre(src)
                    link(normed(h0[:]))
                    link(V.tensor_tensor(h0[:], h0[:], vec4(V_GAMMA), ALU.mult))
                    link(V.tensor_tensor(h0[:], h0[:], vec4(V_BETA), ALU.add))
                    link(V.scalar_tensor_tensor(h0[:], feat[RESIDUAL[s]][:, rows, :], 2.0, h0[:], ALU.mult, ALU.add))
                    centre(h0[:])
                    last = normed(dst)
                elif s in (2, 3):
                    last = V.tensor_tensor(dst, src, vec4(V_B0 + s - 2), ALU.add)
                elif s == 4:
                    link(V.tensor_tensor(h0[:], src, vec4(V_B2), ALU.add))
                    link(V.tensor_tensor(h0[:], h0[:], feat[RESIDUAL[s]][:, rows, :], ALU.add))
                    centre(h0[:])
                    last = normed(dst)
                elif s == 5:
                    x2 = feat[RESIDUAL[s]][:, rows, :]
                    link(V.tensor_tensor(h0[:], src, x2, ALU.mult))
                    link(V.tensor_reduce(s4[:], h0[:], AX.X, ALU.add))
                    link(V.tensor_scalar(h2[:], x2, 0.9, 1.0, ALU.mult, ALU.add))
                    link(V.scalar_tensor_tensor(h0[:], bcast4(s4[:]), -0.01, h2[:], ALU.mult, ALU.add))
                    centre(h0[:])
                    last = normed(dst)
                else:
                    link(V.tensor_tensor(h0[:], src, bcast4(rdeg[:, rows]), ALU.mult))
                    link(V.tensor_tensor(h0[:], h0[:], nat[n % 2][:, 1], ALU.add))
                    link(V.tensor_tensor(h0[:], h0[:], feat[RESIDUAL[s]][:, rows, :], ALU.add))
                    centre(h0[:])
                    last = normed(dst)
                last.then_inc(x_ready, 1)
                dve.wait_ge(x_ready, n + 1)

            dve.wait_ge(inputs_loaded, 16 * N_INPUTS)
            link(V.tensor_tensor(pp_sb[:], par_sb[:, 0:4:2], par_sb[:, 1:4:2], ALU.mult))
            UT = USERS // P
            link(V.tensor_scalar(dg_sb[:, 0:UT], dg_sb[:, 0:UT], pp_sb[:, 0:1], None, ALU.mult))
            link(V.tensor_scalar(dg_sb[:, UT:NT], dg_sb[:, UT:NT], pp_sb[:, 1:2], None, ALU.mult))
            for g in range(NT // 8):
                rows = slice(8 * g, 8 * g + 8)
                bank = dense_banks[g].rearrange("p (t d) -> p t d", d=D)
                dve.wait_ge(dense_done, g + 1)
                link(V.tensor_tensor(bank, bank, dg_sb[:, rows].unsqueeze(2).to_broadcast([P, 8, D]), ALU.mult))
                V.tensor_tensor(feat[OPERAND[0]][:, rows, :], bank, feat[X_BUF][:, rows, :], ALU.add).then_inc(e_ready, 1)
            dve.wait_ge(e_ready, NT // 8)

            for k, st in enumerate(steps):
                s, n = st["sweep"], st["n"]
                if k in rowsum_number:
                    if st["source"] == "turned":
                        dve.wait_ge(turn_row_copied, (st["turn"] + 1) * TC)
                        a = turned_sb[st["turn"] % 2]
                    else:
                        b = bufs[st["buf"]]
                        dve.wait_ge(slot_loaded[b["slot"]], 16 * b["loads"])
                        a = slot_sb[b["slot"]][:]
                    V.tensor_reduce(rowsum[:, st["I"], st["J"] * TC:(st["J"] + 1) * TC], a, AX.X, ALU.add).then_inc(rowsums_done, 1)
                if this_end.get(k) == n:
                    dve.wait_ge(steps_done, k + 1)
                    if n >= 2:
                        dve.wait_ge(projected, n - 1)
                    copy = acc_sb[n % 2]
                    earlier = result_of(s - 1, row_chunk(n)) if s > 0 else None
                    if earlier in next_number:
                        dve.wait_ge(partial_saved, next_number[earlier] + 1)
                        ins = V.tensor_tensor(copy[:], acc[n % 2][:], partial[:, row_chunk(n), :], ALU.add)
                    else:
                        ins = V.tensor_copy(copy[:], acc[n % 2][:])
                    if n in both_chunk:
                        link(ins)
                        mine = halves(s)[1]
                        ins = V.tensor_tensor(copy[mine, :], copy[mine, :], acc_next[next_number[n] % 2][mine, :], ALU.add)
                    ins.then_inc(acc_copied, 1)
                    dve.wait_ge(acc_copied, n + 1)
                if k in save_after:
                    m_of = save_after[k]
                    m = next_number[m_of]
                    dve.wait_ge(steps_done, k + 1)
                    i = row_chunk(m_of)
                    if m_of in both_chunk:
                        _, mine, others = halves(s)
                        link(V.memset(partial[mine, i, :], 0.0))
                        ins = V.tensor_copy(partial[others, i, :], acc_next[m % 2][others, :])
                    else:
                        ins = V.tensor_copy(partial[:, i, :], acc_next[m % 2][:])
                    ins.then_inc(partial_saved, 1)
                if s == SWEEPS - 1 and ends[n, THIS][0] == k:
                    c = n - (SWEEPS - 1) * NC
                    dve.wait_ge(x3_transposed, c + 1)
                    dve.wait_ge(projected, n)
                    V.tensor_copy(x3T, tr[0][0:D, :]).then_inc(x3T_copied, 1)
                for m in project_after.get(k, []):
                    finish(m)
                if k == ends[NC, THIS][1]:
                    dve.wait_ge(rowsums_done, NC * NC)
                    link(V.tensor_reduce(rdeg[:], rowsum.rearrange("p c t -> p t c"), AX.X, ALU.add))
                    link(V.tensor_scalar(rdeg[:], rdeg[:], 1.0, None, ALU.add))
                    link(V.reciprocal(rdeg[:], rdeg[:]))


def kernel(**inputs):
    import numpy as np
    import concourse.bacc as bacc
    from concourse.bass_utils import run_bass_kernel_spmd

    a = {k: np.asarray(v) for k, v in inputs.items()}
    A = a["adj"]

    def blocks(m):
        return np.ascontiguousarray(m.reshape(NC, TC, P, NC, C).transpose(3, 0, 2, 1, 4))

    def tiled(v):
        return np.ascontiguousarray(np.moveaxis(v.reshape(NT, P, *v.shape[1:]), 0, 1))

    L3 = a["L3_gnn_W"]
    weights = np.ascontiguousarray(np.stack([
        a["L0_gnn_W_u"], a["L0_gnn_W_i"], a["L1_gnn_W0"].T, a["L1_gnn_W1"].T, a["L1_gnn_W2"].T,
        L3[:, :D].T, L3[:, D:].T, np.eye(D, dtype=np.float32)], axis=1))
    vecs = np.ascontiguousarray(np.broadcast_to(np.stack([
        a["L0_gnn_ln_gamma"], a["L0_gnn_ln_beta"], a["L1_gnn_b0"], a["L1_gnn_b1"], a["L1_gnn_b2"]]), (P, 5, D)))
    par = np.ascontiguousarray(np.broadcast_to(np.concatenate([a["L0_gnn_par_u"], a["L0_gnn_par_i"]]), (P, 4)))
    arrays = {
        "A_natural": blocks(A), "A_transposed": blocks(A.T),
        "x": tiled(a["x"]), "weights": weights, "vecs": vecs,
        "diag": tiled(np.concatenate([a["L0_gnn_diag_u"], a["L0_gnn_diag_i"]])), "par": par,
        "eye": np.eye(P, dtype=np.float32),
    }
    nc = bacc.Bacc("TRN2", target_bir_lowering=False, num_devices=1)
    args = [nc.dram_tensor(f"in_{k}", v.shape, mybir.dt.float32, kind="ExternalInput").ap() for k, v in arrays.items()]
    out = nc.dram_tensor("out", (P, NT, D), mybir.dt.float32, kind="ExternalOutput").ap()
    layers_kernel(nc, out, *args)
    r = run_bass_kernel_spmd(nc, [{f"in_{k}": v for k, v in arrays.items()}], core_ids=[0])
    got = r.results[0]["out"]
    return np.ascontiguousarray(np.moveaxis(got, 0, 1)).reshape(N, D)
```

```python
import concourse.bass as bass
from concourse import mybir
from contextlib import ExitStack

N = 5120
D = 64
P = 128
C = 512
NC = N // C
TC = C // P
NT = N // P
USERS = 2048
EPS = 1e-5
SLOTS = 8
BLOCK = TC * C

THIS, NEXT, BOTH, TURN = 0, 1, 2, 3
SWEEPS = 7
UP, DOWN = list(range(NC)), list(range(NC))[::-1]
ORDER = {0: UP, 1: UP, 2: DOWN, 3: UP, 4: DOWN, 5: UP, 6: [0, 9, 1, 8, 2, 7, 3, 6, 5, 4]}
MATRIX = {0: "A", 1: "A", 2: "W", 3: "W", 4: "W", 5: "A", 6: "A", 7: None}
LAG = {1: 2, 2: 4, 3: 4, 4: 2, 5: 4}
LAG_SQUARE = 2
SETTLED = 3
SETTLED_END = NC - 1
EARLY = (5, 6, 7, 8, 9)
EARLY_LOADS = {(4, 3): 5, (5, 3): 6, (6, 5): 7, (7, 5): 8, (8, 5): 9}
KEPT_LOADS = {(0, 3): 0, (0, 4): 1, (0, 6): 2, (1, 1): 3, (1, 4): 4, (2, 3): 5, (3, 3): 6, (4, 3): 7, (5, 3): 8, (6, 3): 9}

W_USER, W_ITEM, W_L1_0, W_L1_1, W_L1_2, W_SELF, W_NEIGH = range(7)
PROJECT = {2: W_L1_0, 3: W_L1_1, 4: W_L1_2, 6: W_NEIGH}
V_GAMMA, V_BETA, V_B0, V_B1, V_B2 = range(5)
OPERAND = {0: 0, 1: 2, 2: 0, 3: 1, 4: 2, 5: 1, 6: 0, 7: 2}
RESIDUAL = {1: 1, 4: 0, 5: 1, 6: 0}
X_BUF = 1


def blocks_of(s):
    order = ORDER[s]
    for k, i in enumerate(order):
        done, ahead = order[:k], order[k + 1:]
        if s == 0:
            js = list(range(NC))
        elif s == 1:
            js = [i] + ahead[::-1] + done
        elif s < SWEEPS - 1:
            js = [i] + done
        else:
            js = list(range(i, NC))
        yield k, i, js, done if 0 < s < SWEEPS - 1 else []


def plan():
    steps, bufs, issue, turns = [], [], [], []

    def add(s, k, i, j, part, source, buf=None, turn=None, squared=False):
        steps.append(dict(sweep=s, I=i, J=j, part=part, n=s * NC + k, source=source, buf=buf, turn=turn,
                          squared=squared))
        q = len(steps) - 1
        if buf is not None:
            bufs[buf]["last"] = q
            bufs[buf].setdefault("use", q)
            of = bufs[buf].get("of")
            if of is not None:
                bufs[of]["last"] = max(bufs[of].get("last", 0), q)

    def load(s, i, j):
        bufs.append(dict(kind="load", s=s, I=i, J=j))
        issue.append(("slot", len(bufs) - 1))
        return len(bufs) - 1

    early = {}
    for k, i, js, _ in blocks_of(0):
        turned = [i] + ([0] if i in EARLY else [])
        natural = [j for j in js if j not in turned]
        waiting = []
        for at, j in enumerate(natural):
            buf = load(0, i, j)
            if (k, at) in KEPT_LOADS:
                issue.append(("kept", KEPT_LOADS[k, at]))
            if (k, at) in EARLY_LOADS:
                col = EARLY_LOADS[k, at]
                early[col] = load(1, 0, col)
            add(0, k, i, j, THIS, "slot", buf)
            if at in (1, 4) and turned:
                j = turned.pop(0)
                turns.append(dict(I=j, J=i, buf=None if j == i else early[i]))
                turn = len(turns) - 1
                turns[turn]["step"] = len(steps)
                add(0, k, i, j, TURN, "kept" if j == i else "slot", turns[turn]["buf"], turn)
                waiting.append((at + 2, j, turn))
            if waiting and waiting[0][0] == at:
                _, j, turn = waiting.pop(0)
                add(0, k, i, j, THIS, "turned", turn=turn)

    for s in range(1, SWEEPS):
        this_w, next_w = MATRIX[s] == "W", MATRIX[s + 1] == "W"
        later, at = [], 0
        for k, i, js, shared in blocks_of(s):
            for j in js:
                kept = i == j
                if s == 1 and i == 0 and j in early:
                    own = early[j]
                else:
                    own = None if kept else load(s, i, j)
                here = "kept" if kept else "slot"
                both = j in shared and this_w == next_w and SETTLED <= k < SETTLED_END
                next_first = j in shared and this_w and not next_w and SETTLED <= k < SETTLED_END
                if both:
                    add(s, k, i, j, BOTH, here, own, squared=this_w)
                elif next_first:
                    add(s, k, i, j, NEXT, here, own)
                    later.append((at + LAG_SQUARE, dict(k=k, i=i, j=j, part=THIS, source="slot", buf=own, squared=True)))
                else:
                    this = own
                    if this_w and not (own is not None and next_w):
                        bufs.append(dict(kind="square", of=own, I=i))
                        this = len(bufs) - 1
                    if SETTLED <= k < SETTLED_END and this_w and not next_w:
                        later.append((at + LAG_SQUARE, dict(k=k, i=i, j=j, part=THIS, source="slot", buf=this, squared=True)))
                    else:
                        add(s, k, i, j, THIS, "slot" if this is not None else here, this, squared=this_w)
                    if j in shared:
                        later.append((at + LAG[s], dict(k=k, i=i, j=j, part=NEXT, source="slot", buf=own, squared=next_w)))
                while later and at >= later[0][0]:
                    add(s, **later.pop(0)[1])
                at += 1
        for _, st in later:
            add(s, **st)

    ends = {}
    for q, st in enumerate(steps):
        if st["part"] != TURN:
            for part in ((THIS, NEXT) if st["part"] == BOTH else (st["part"],)):
                ends.setdefault((st["n"], part), [q, q])[1] = q

    held = [None] * SLOTS
    loads = [0] * SLOTS
    for k, b in enumerate(bufs):
        slot = min(range(SLOTS), key=lambda q: -1 if held[q] is None else bufs[held[q]]["last"])
        b["slot"], b["before"] = slot, held[slot]
        assert b["before"] is None or bufs[b["before"]]["last"] < b["use"]
        held[slot] = k
        loads[slot] += b["kind"] == "load"
        b["loads"] = loads[slot]
    return steps, bufs, issue, turns, ends


def layers_kernel(nc, out, Anat, At, x, weights, vecs, diag, par, eye):
    f32 = mybir.dt.float32
    ALU = mybir.AluOpType
    ACT = mybir.ActivationFunctionType
    AX = mybir.AxisListType

    steps, bufs, issue, turns, ends = plan()
    n_chunks = SWEEPS * NC

    squares, square_of = [], {}
    for k, st in enumerate(steps):
        buf = st["buf"]
        if st["squared"] and buf not in square_of:
            square_of[buf] = len(squares)
            if bufs[buf]["kind"] == "square":
                squares.append((bufs[buf]["of"], st["I"], buf, None))
            else:
                before = [q for q in range(k) if steps[q]["buf"] == buf]
                squares.append((buf, None, buf, before[-1] if before else None))

    def row_chunk(n):
        return ORDER[n // NC][n % NC]

    def result_of(s, i):
        return s * NC + ORDER[s].index(i)

    def needs(st):
        if st["part"] == TURN:
            return -1
        s = st["sweep"] - (st["part"] == THIS)
        return result_of(s, st["J"]) if s >= 0 else -1

    project_after = {}
    for n in range(n_chunks):
        k = ends[n, THIS][1]
        if k + 1 < len(steps) and needs(steps[k + 1]) != n:
            k += 1
        project_after.setdefault(k, []).append(n)
    this_end = {ends[n, THIS][1]: n for n in range(n_chunks)}
    next_end = {q[1]: n for (n, part), q in ends.items() if part == NEXT}
    next_number = {n: m for m, (_, n) in enumerate(sorted(next_end.items()))}
    save_after = {max(k, ends[n, THIS][1]): n for k, n in next_end.items()}
    both_chunk = {st["n"] for st in steps if st["part"] == BOTH}
    rowsum_number = {k: q for q, k in enumerate(k for k, st in enumerate(steps) if st["sweep"] == 0 and st["source"] == "slot" and st["part"] == THIS)}
    rowsum_of_buf = {steps[k]["buf"]: q for k, q in rowsum_number.items()}
    turned_use = {st["turn"]: k for k, st in enumerate(steps) if st["source"] == "turned"}

    def halves(s):
        t, x = OPERAND[s], OPERAND[s + 1]
        low, high = slice(0, D), slice(D, P)
        assert abs(t - x) == 1
        return (t, low, high) if t < x else (x, high, low)

    ctx = ExitStack()
    with ctx:
        def sb(name, shape):
            return ctx.enter_context(nc.sbuf_tensor(name, shape, f32))

        def ps(name, shape):
            return ctx.enter_context(nc.psum_tensor(name, shape, f32))

        def sem(name):
            return ctx.enter_context(nc.semaphore(name))

        slot_sb = [sb(f"slot{q}", [P, TC, C]) for q in range(SLOTS)]
        diag_sb = [sb(f"diagonal{i}", [P, TC, C]) for i in range(NC)]
        feats = sb("features", [P, NT, 3, D])
        feat = [feats[:, :, q, :] for q in range(3)]
        partial = sb("partial", [P, NC, C])
        acc_sb = [sb(f"acc_sb{q}", [P, C]) for q in range(2)]
        w_sb = sb("weights_sb", [P, 7, D])
        v_sb = sb("vectors_sb", [P, 5, D])
        dg_sb = sb("row_scale", [P, NT])
        par_sb = sb("par_sb", [P, 4])
        pp_sb = sb("par_product", [P, 2])
        eye_sb = sb("eye_sb", [P, P])
        spare = sb("rowsums_then_x3T", [P, C])
        rowsum = spare[:, 0:NC * NT].rearrange("p (c t) -> p c t", c=NC)
        rdeg = sb("rdeg", [P, NT])
        h0 = sb("work0", [P, TC, D])
        h1 = sb("work1", [P, TC, D])
        h2 = sb("work2", [P, TC, D])
        s4 = sb("row_sum", [P, TC])
        v4 = sb("row_square_sum", [P, TC])
        r4 = sb("row_rstd", [P, TC])
        minus_half = sb("minus_half", [P, TC])
        xT_sb = partial[0:D, :, :].rearrange("p c n -> p (c n)")
        turned_sb = [partial[:, q * TC:(q + 1) * TC, :] for q in range(2)]
        x3T = spare[0:D, :]

        acc = [ps(f"acc{q}", [P, C]) for q in range(2)]
        acc_next = [ps(f"acc_next{q}", [P, C]) for q in range(2)]
        nat = [ps(f"nat{q}", [P, 2, TC, D]) for q in range(2)]
        nat_halves = [b[:].rearrange("p a t d -> p (a t d)").rearrange("p (t e) -> p t e", t=TC) for b in nat]
        tr = [ps(f"transposed{q}", [P, C]) for q in range(2)]
        turn_banks = [acc_next[0], acc_next[1], tr[0], tr[1]]

        slot_loaded = [sem(f"slot{q}_loaded") for q in range(SLOTS)]
        diag_loaded = [sem(f"diagonal{i}_loaded") for i in range(NC)]
        inputs_loaded = sem("inputs_loaded")
        x_loaded = sem("x_loaded")
        x_transposed = sem("x_transposed")
        xT_copied = sem("xT_copied")
        steps_done = sem("steps_done")
        squares_done = sem("squares_done")
        rowsums_done = sem("rowsums_done")
        dense_done = sem("dense_done")
        e_ready = sem("e_ready")
        acc_copied = sem("acc_copied")
        partial_saved = sem("partial_saved")
        projected = sem("projected")
        x_ready = sem("x_ready")
        var_ready = sem("var_ready")
        rstd_ready = sem("rstd_ready")
        exponent_ready = sem("exponent_ready")
        turn_row_done = sem("turn_row_done")
        turn_row_copied = sem("turn_row_copied")
        x3_transposed = sem("x3_transposed")
        x3T_copied = sem("x3T_copied")
        dve_step = sem("dve_step")
        out_stored = sem("out_stored")
        N_INPUTS = 6

        def bcast4(ap):
            return ap.unsqueeze(2).to_broadcast([P, TC, D])

        def vec4(v):
            return v_sb[:, v, :].unsqueeze(1).to_broadcast([P, TC, D])

        x_parts = [(diag_sb[NC - 2][:].rearrange("p t (q d) -> p (t q) d", d=D), slice(0, BLOCK // D)),
                   (diag_sb[NC - 1][:].rearrange("p t (q d) -> p (t q) d", d=D)[:, 0:NT - BLOCK // D, :], slice(BLOCK // D, NT))]

        def x_tiles(first, end):
            part, rows = x_parts[first >= BLOCK // D]
            return part[:, first - rows.start:end - rows.start, :]

        dense_banks = [acc[0][:], acc[1][:], nat[0][:].rearrange("p a t d -> p (a t d)"),
                       nat[1][:].rearrange("p a t d -> p (a t d)"), acc_next[0][:]]

        block = ctx.enter_context(nc.Block())

        @block.sync
        def _(sp):
            for part, rows in x_parts:
                sp.dma_start(part, x[:, rows, :]).then_inc(x_loaded, 16)
            sp.dma_start(eye_sb[:], eye).then_inc(inputs_loaded, 16)
            sp.dma_start(w_sb[0:D], weights).then_inc(inputs_loaded, 16)
            sp.dma_start(w_sb[D:P], weights).then_inc(inputs_loaded, 16)
            sp.dma_start(v_sb[:], vecs).then_inc(inputs_loaded, 16)
            sp.dma_start(dg_sb[:], diag).then_inc(inputs_loaded, 16)
            sp.dma_start(par_sb[:], par).then_inc(inputs_loaded, 16)
            for what, k in issue:
                if what == "kept":
                    if k >= NC - 2:
                        sp.wait_ge(e_ready, NT // 8)
                    sp.dma_start(diag_sb[k][:], At[k, k]).then_inc(diag_loaded[k], 16)
                    continue
                b = bufs[k]
                if b["before"] is not None:
                    sp.wait_ge(steps_done, bufs[b["before"]]["last"] + 1)
                    if b["before"] in rowsum_of_buf:
                        sp.wait_ge(rowsums_done, rowsum_of_buf[b["before"]] + 1)
                source = Anat if b["s"] == 0 else At
                sp.dma_start(slot_sb[b["slot"]][:], source[b["I"], b["J"]]).then_inc(slot_loaded[b["slot"]], 16)

        @block.scalar
        def _(act):
            for g in range(NT // 8):
                for h in range(2):
                    act.wait_ge(x_transposed, 2 * g + h + 1)
                    nc.scalar.copy(xT_sb[:, (2 * g + h) * C:(2 * g + h + 1) * C], turn_banks[(2 * g + h) % 4][0:D, :]).then_inc(xT_copied, 1)
            for t in range(len(turns)):
                if t >= 2:
                    act.wait_ge(steps_done, turned_use[t - 2] + 1)
                for r in range(TC):
                    if r < TC - 1:
                        act.wait_ge(turn_row_done, t * (TC - 1) + r + 1)
                    else:
                        act.wait_ge(steps_done, turns[t]["step"] + 1)
                    tile = turns[t]["I"] * TC + r
                    nc.scalar.activation(turned_sb[t % 2][:, r, :], turn_banks[r][:], ACT.Copy,
                                         accum_out=rowsum[:, turns[t]["J"], tile:tile + 1]).then_inc(turn_row_copied, 1)
            for src, diag_i, dst, before in squares:
                if src is None:
                    act.wait_ge(diag_loaded[diag_i], 16)
                    source = diag_sb[diag_i]
                else:
                    act.wait_ge(slot_loaded[bufs[src]["slot"]], 16 * bufs[src]["loads"])
                    source = slot_sb[bufs[src]["slot"]]
                if before is not None:
                    act.wait_ge(steps_done, before + 1)
                if dst != src:
                    act.wait_ge(steps_done, bufs[bufs[dst]["before"]]["last"] + 1)
                nc.scalar.activation(slot_sb[bufs[dst]["slot"]][:], source[:], ACT.Square).then_inc(squares_done, 1)
            for c, i in enumerate(ORDER[SWEEPS - 1]):
                act.wait_ge(x_ready, (SWEEPS - 1) * NC + c + 1)
                act.dma_start(out[:, i * TC:(i + 1) * TC, :], feat[OPERAND[SWEEPS]][:, i * TC:(i + 1) * TC, :]).then_inc(out_stored, 16)
            act.wait_ge(out_stored, 16 * NC)

        @block.gpsimd
        def _(pool):
            nc.gpsimd.memset(minus_half[:], -0.5).then_inc(exponent_ready, 1)
            pool.wait_ge(exponent_ready, 1)
            for k in range(5 * NC):
                pool.wait_ge(var_ready, k + 1)
                nc.gpsimd.tensor_tensor(r4[:], v4[:], minus_half[:], ALU.pow).then_inc(rstd_ready, 1)

        @block.tensor
        def _(pe):
            pe.wait_ge(inputs_loaded, 16 * N_INPUTS)
            pe.wait_ge(x_loaded, 32)
            for c in range(NC):
                if c >= 4:
                    pe.wait_ge(xT_copied, c - 3)
                for q in range(TC):
                    last = nc.tensor.transpose(turn_banks[c % 4][0:D, q * P:(q + 1) * P], x_tiles(c * TC + q, c * TC + q + 1)[:, 0, :], eye_sb[:])
                last.then_inc(x_transposed, 1)
            for g in range(NT // 8):
                pe.wait_ge(xT_copied, 2 * g + 2)
                for q in range(8):
                    t = 8 * g + q
                    w = W_USER if t < USERS // P else W_ITEM
                    last = nc.tensor.matmul(dense_banks[g][:, q * D:(q + 1) * D], xT_sb[:, t * P:(t + 1) * P],
                                            w_sb[0:D, w, :], start=True, stop=True)
                last.then_inc(dense_done, 1)

            pe.wait_ge(e_ready, NT // 8)
            known = 0
            for k, st in enumerate(steps):
                s, n, part = st["sweep"], st["n"], st["part"]
                first = [p for p in (THIS, NEXT) if ends.get((n, p), (None,))[0] == k]
                if needs(st) + 1 > known:
                    known = needs(st) + 1
                    pe.wait_ge(x_ready, known)
                if st["source"] == "kept":
                    pe.wait_ge(diag_loaded[st["J"]], 16)
                    a = diag_sb[st["J"]]
                elif st["source"] == "turned":
                    pe.wait_ge(turn_row_copied, (st["turn"] + 1) * TC)
                    a = turned_sb[st["turn"] % 2]
                else:
                    b = bufs[st["buf"]]
                    a = slot_sb[b["slot"]]
                    if st["squared"]:
                        pe.wait_ge(squares_done, square_of[st["buf"]] + 1)
                    else:
                        pe.wait_ge(slot_loaded[b["slot"]], 16 * b["loads"])
                if part == TURN:
                    for r in range(TC):
                        if st["turn"] > 0:
                            pe.wait_ge(turn_row_copied, (st["turn"] - 1) * TC + r + 1)
                        for q in range(TC):
                            last = nc.tensor.transpose(turn_banks[r][:, q * P:(q + 1) * P], a[:, q, r * P:(r + 1) * P], eye_sb[:])
                        if r < TC - 1:
                            last.then_inc(turn_row_done, 1)
                if THIS in first and n >= 2:
                    pe.wait_ge(acc_copied, n - 1)
                if NEXT in first:
                    m = next_number[n]
                    if m >= 2:
                        pe.wait_ge(partial_saved, m - 1)
                if part == BOTH:
                    low, _, _ = halves(s)
                    bank = acc_next[next_number[n] % 2]
                    for q in range(TC):
                        last = nc.tensor.matmul(bank[:], feats[:, st["J"] * TC + q, low:low + 2, :].rearrange("p b d -> p (b d)"), a[:, q, :],
                                                start=NEXT in first and q == 0, stop=q == TC - 1 and next_end.get(k) == n)
                elif part in (THIS, NEXT):
                    bank = acc[n % 2] if part == THIS else acc_next[next_number[n] % 2]
                    x_op = feat[OPERAND[s + part]]
                    ends_here = (this_end if part == THIS else next_end).get(k) == n
                    if part == THIS and n in both_chunk:
                        ends_here = True
                    for q in range(TC):
                        half = slice(D * (q % 2), D * (q % 2) + D)
                        last = nc.tensor.matmul(bank[half, :], x_op[:, st["J"] * TC + q, :], a[:, q, :],
                                                start=part in first and q < 2, stop=ends_here and q >= 2)
                last.then_inc(steps_done, 1)

                if s == SWEEPS - 1 and THIS in first:
                    if n > (SWEEPS - 1) * NC:
                        pe.wait_ge(x3T_copied, n - (SWEEPS - 1) * NC)
                    for q in range(TC):
                        last = nc.tensor.transpose(tr[0][0:D, q * P:(q + 1) * P], feat[OPERAND[s]][:, st["I"] * TC + q, :], eye_sb[:])
                    last.then_inc(x3_transposed, 1)

                for m in project_after.get(k, []):
                    ms = m // NC
                    pe.wait_ge(acc_copied, m + 1)
                    if m >= 2:
                        pe.wait_ge(x_ready, m - 1)
                    for q in range(TC):
                        rows_q = acc_sb[m % 2][:, q * P:(q + 1) * P]
                        if ms in PROJECT:
                            last = nc.tensor.matmul(nat[m % 2][:, 0, q, :], rows_q, w_sb[:, PROJECT[ms], :], start=True, stop=True)
                        else:
                            last = nc.tensor.transpose(nat_halves[m % 2][:, q, :], rows_q, eye_sb[:])
                    if ms == SWEEPS - 1:
                        mc = m - (SWEEPS - 1) * NC
                        pe.wait_ge(x3T_copied, mc + 1)
                        for q in range(TC):
                            last = nc.tensor.matmul(nat[m % 2][:, 1, q, :], x3T[:, q * P:(q + 1) * P],
                                                    w_sb[0:D, W_SELF, :], start=True, stop=True)
                    last.then_inc(projected, 1)

        @block.vector
        def _(dve):
            chain = [0]
            norms = [0]

            def link(ins):
                chain[0] += 1
                ins.then_inc(dve_step, 1)
                dve.wait_ge(dve_step, chain[0])

            V = nc.vector

            def centre(src):
                link(V.tensor_reduce(s4[:], src, AX.X, ALU.add))
                link(V.scalar_tensor_tensor(h1[:], bcast4(s4[:]), -1.0 / D, src, ALU.mult, ALU.add))
                link(V.tensor_tensor(h2[:], h1[:], h1[:], ALU.mult))
                norms[0] += 1
                link(V.tensor_reduce(s4[:], h2[:], AX.X, ALU.add))
                V.tensor_scalar(v4[:], s4[:], D * EPS, None, ALU.add).then_inc(var_ready, 1)
                dve.wait_ge(rstd_ready, norms[0])

            def normed(dst):
                return V.scalar_tensor_tensor(dst, h1[:], float(D) ** 0.5, bcast4(r4[:]), ALU.mult, ALU.mult)

            def finish(n):
                s = n // NC
                i = row_chunk(n)
                rows = slice(i * TC, (i + 1) * TC)
                src = nat[n % 2][:, 0]
                dst = feat[OPERAND[s + 1]][:, rows, :]
                dve.wait_ge(projected, n + 1)
                if s not in PROJECT:
                    both = nat_halves[n % 2].rearrange("p t (h d) -> p t d h", h=2)
                if s == 0:
                    last = V.tensor_reduce(dst, both, AX.X, ALU.add)
                elif s == 1:
                    link(V.tensor_reduce(h0[:], both, AX.X, ALU.add))
                    centre(h0[:])
                    link(normed(h0[:]))
                    link(V.tensor_tensor(h0[:], h0[:], vec4(V_GAMMA), ALU.mult))
                    link(V.tensor_tensor(h0[:], h0[:], vec4(V_BETA), ALU.add))
                    link(V.scalar_tensor_tensor(h0[:], feat[RESIDUAL[s]][:, rows, :], 2.0, h0[:], ALU.mult, ALU.add))
                    centre(h0[:])
                    last = normed(dst)
                elif s in (2, 3):
                    last = V.tensor_tensor(dst, src, vec4(V_B0 + s - 2), ALU.add)
                elif s == 4:
                    link(V.tensor_tensor(h0[:], src, vec4(V_B2), ALU.add))
                    link(V.tensor_tensor(h0[:], h0[:], feat[RESIDUAL[s]][:, rows, :], ALU.add))
                    centre(h0[:])
                    last = normed(dst)
                elif s == 5:
                    x2 = feat[RESIDUAL[s]][:, rows, :]
                    link(V.tensor_reduce(h0[:], both, AX.X, ALU.add))
                    link(V.tensor_tensor(h0[:], h0[:], x2, ALU.mult))
                    link(V.tensor_reduce(s4[:], h0[:], AX.X, ALU.add))
                    link(V.tensor_scalar(h2[:], x2, 0.9, 1.0, ALU.mult, ALU.add))
                    link(V.scalar_tensor_tensor(h0[:], bcast4(s4[:]), -0.01, h2[:], ALU.mult, ALU.add))
                    centre(h0[:])
                    last = normed(dst)
                else:
                    link(V.tensor_tensor(h0[:], src, bcast4(rdeg[:, rows]), ALU.mult))
                    link(V.tensor_tensor(h0[:], h0[:], nat[n % 2][:, 1], ALU.add))
                    link(V.tensor_tensor(h0[:], h0[:], feat[RESIDUAL[s]][:, rows, :], ALU.add))
                    centre(h0[:])
                    last = normed(dst)
                last.then_inc(x_ready, 1)
                dve.wait_ge(x_ready, n + 1)

            dve.wait_ge(x_loaded, 32)
            for part, rows in x_parts:
                link(V.tensor_copy(feat[X_BUF][:, rows, :], part))
            dve.wait_ge(inputs_loaded, 16 * N_INPUTS)
            link(V.tensor_tensor(pp_sb[:], par_sb[:, 0:4:2], par_sb[:, 1:4:2], ALU.mult))
            UT = USERS // P
            link(V.tensor_scalar(dg_sb[:, 0:UT], dg_sb[:, 0:UT], pp_sb[:, 0:1], None, ALU.mult))
            link(V.tensor_scalar(dg_sb[:, UT:NT], dg_sb[:, UT:NT], pp_sb[:, 1:2], None, ALU.mult))
            for g in range(NT // 8):
                rows = slice(8 * g, 8 * g + 8)
                bank = dense_banks[g].rearrange("p (t d) -> p t d", d=D)
                dve.wait_ge(dense_done, g + 1)
                link(V.tensor_tensor(bank, bank, dg_sb[:, rows].unsqueeze(2).to_broadcast([P, 8, D]), ALU.mult))
                V.tensor_tensor(feat[OPERAND[0]][:, rows, :], bank, x_tiles(rows.start, rows.stop), ALU.add).then_inc(e_ready, 1)
            dve.wait_ge(e_ready, NT // 8)

            for k, st in enumerate(steps):
                s, n = st["sweep"], st["n"]
                if k in rowsum_number:
                    b = bufs[st["buf"]]
                    dve.wait_ge(slot_loaded[b["slot"]], 16 * b["loads"])
                    V.tensor_reduce(rowsum[:, st["I"], st["J"] * TC:(st["J"] + 1) * TC], slot_sb[b["slot"]][:], AX.X, ALU.add).then_inc(rowsums_done, 1)
                if this_end.get(k) == n:
                    dve.wait_ge(steps_done, k + 1)
                    if n >= 2:
                        dve.wait_ge(projected, n - 1)
                    copy = acc_sb[n % 2]
                    earlier = result_of(s - 1, row_chunk(n)) if s > 0 else None
                    if earlier in next_number:
                        dve.wait_ge(partial_saved, next_number[earlier] + 1)
                        ins = V.tensor_tensor(copy[:], acc[n % 2][:], partial[:, row_chunk(n), :], ALU.add)
                    else:
                        ins = V.tensor_copy(copy[:], acc[n % 2][:])
                    if n in both_chunk:
                        link(ins)
                        mine = halves(s)[1]
                        ins = V.tensor_tensor(copy[mine, :], copy[mine, :], acc_next[next_number[n] % 2][mine, :], ALU.add)
                    ins.then_inc(acc_copied, 1)
                    dve.wait_ge(acc_copied, n + 1)
                if k in save_after:
                    m_of = save_after[k]
                    m = next_number[m_of]
                    dve.wait_ge(steps_done, k + 1)
                    i = row_chunk(m_of)
                    if m_of in both_chunk:
                        _, mine, others = halves(s)
                        link(V.memset(partial[mine, i, :], 0.0))
                        ins = V.tensor_copy(partial[others, i, :], acc_next[m % 2][others, :])
                    else:
                        ins = V.tensor_copy(partial[:, i, :], acc_next[m % 2][:])
                    ins.then_inc(partial_saved, 1)
                if s == SWEEPS - 1 and ends[n, THIS][0] == k:
                    c = n - (SWEEPS - 1) * NC
                    dve.wait_ge(x3_transposed, c + 1)
                    dve.wait_ge(projected, n)
                    V.tensor_copy(x3T, tr[0][0:D, :]).then_inc(x3T_copied, 1)
                for m in project_after.get(k, []):
                    finish(m)
                if k == ends[NC, THIS][1]:
                    dve.wait_ge(rowsums_done, len(rowsum_number))
                    dve.wait_ge(turn_row_copied, len(turns) * TC)
                    link(V.tensor_reduce(rdeg[:], rowsum.rearrange("p c t -> p t c"), AX.X, ALU.add))
                    link(V.tensor_scalar(rdeg[:], rdeg[:], 1.0, None, ALU.add))
                    link(V.reciprocal(rdeg[:], rdeg[:]))


def kernel(**inputs):
    import numpy as np
    import concourse.bacc as bacc
    from concourse.bass_utils import run_bass_kernel_spmd

    a = {k: np.asarray(v) for k, v in inputs.items()}
    A = a["adj"]

    def blocks(m):
        return np.ascontiguousarray(m.reshape(NC, TC, P, NC, C).transpose(3, 0, 2, 1, 4))

    def tiled(v):
        return np.ascontiguousarray(np.moveaxis(v.reshape(NT, P, *v.shape[1:]), 0, 1))

    L3 = a["L3_gnn_W"]
    weights = np.ascontiguousarray(np.stack([
        a["L0_gnn_W_u"], a["L0_gnn_W_i"], a["L1_gnn_W0"].T, a["L1_gnn_W1"].T, a["L1_gnn_W2"].T,
        L3[:, :D].T, L3[:, D:].T], axis=1))
    vecs = np.ascontiguousarray(np.broadcast_to(np.stack([
        a["L0_gnn_ln_gamma"], a["L0_gnn_ln_beta"], a["L1_gnn_b0"], a["L1_gnn_b1"], a["L1_gnn_b2"]]), (P, 5, D)))
    par = np.ascontiguousarray(np.broadcast_to(np.concatenate([a["L0_gnn_par_u"], a["L0_gnn_par_i"]]), (P, 4)))
    arrays = {
        "A_natural": blocks(A), "A_transposed": blocks(A.T),
        "x": tiled(a["x"]), "weights": weights, "vecs": vecs,
        "diag": tiled(np.concatenate([a["L0_gnn_diag_u"], a["L0_gnn_diag_i"]])), "par": par,
        "eye": np.eye(P, dtype=np.float32),
    }
    nc = bacc.Bacc("TRN2", target_bir_lowering=False, num_devices=1)
    args = [nc.dram_tensor(f"in_{k}", v.shape, mybir.dt.float32, kind="ExternalInput").ap() for k, v in arrays.items()]
    out = nc.dram_tensor("out", (P, NT, D), mybir.dt.float32, kind="ExternalOutput").ap()
    layers_kernel(nc, out, *args)
    r = run_bass_kernel_spmd(nc, [{f"in_{k}": v for k, v in arrays.items()}], core_ids=[0])
    got = r.results[0]["out"]
    return np.ascontiguousarray(np.moveaxis(got, 0, 1)).reshape(N, D)
```
